# Optimizing a Trainium2 kernel written in Bass

```python
import numpy as np
import jax
import jax.numpy as jnp

def _softmax(x, axis=-1):
    return jax.nn.softmax(x, axis=axis)

def _gelu(x):
    return jax.nn.gelu(x, approximate=True)

def _silu(x):
    return jax.nn.silu(x)

def _sigmoid(x):
    return jax.nn.sigmoid(x)

def _layernorm(x, axis=-1, eps=1e-05):
    m = jnp.mean(x, axis=axis, keepdims=True)
    v = jnp.var(x, axis=axis, keepdims=True)
    return (x - m) / jnp.sqrt(v + eps)

def _scatter_add(tgt, idx, src, axis=0):
    return tgt.at[idx].add(src)

def _segment_sum(src, seg, n):
    return jax.ops.segment_sum(src, seg, n)
kernel_name = 'mk_rec_standalone_d1_rec_r8_42060e'

def setup_inputs(seed: int=0):
    np.random.seed(seed)
    _w = jnp.asarray

    def _rec_inputs():
        import jax
        import jax.numpy as jnp
        _rk = jax.random.key(seed)
        r_users = jax.random.randint(jax.random.fold_in(_rk, 1), (1024,), 2, 9997, jnp.int32)
        r_items = jax.random.randint(jax.random.fold_in(_rk, 2), (1024,), 23, 99925, jnp.int32)
        return (r_users, r_items)
    r_users, r_items = _rec_inputs()

    def _L0_rec_setup():
        import jax, jax.numpy as jnp
        import numpy as np
        NUM_USERS = 1250
        NUM_ITEMS = 12500
        EMBED_DIM = 64
        BATCH = 512
        key = jax.random.key(seed)
        k1, k2, k3, k4, k5 = jax.random.split(key, 5)
        user_emb = jax.random.normal(k1, (NUM_USERS, EMBED_DIM), dtype=jnp.float32)
        item_emb = jax.random.normal(k2, (NUM_ITEMS, EMBED_DIM), dtype=jnp.float32)
        social_weight = jax.random.normal(k3, (NUM_USERS, NUM_USERS), dtype=jnp.float32)
        users = jax.random.randint(k4, (BATCH,), 0, NUM_USERS, dtype=jnp.int64)
        items = jax.random.randint(k5, (BATCH,), 0, NUM_ITEMS, dtype=jnp.int64)
        return {'user_emb': user_emb, 'item_emb': item_emb, 'social_weight': social_weight, 'users': users, 'items': items}
    _L0_rec_all = _L0_rec_setup()
    _L0_rec_in = {k: v for k, v in _L0_rec_all.items() if k in ('user_emb', 'item_emb', 'social_weight')}
    del _L0_rec_all
    return {'r_users': r_users, 'r_items': r_items, 'L0_rec_user_emb': _L0_rec_in['user_emb'], 'L0_rec_item_emb': _L0_rec_in['item_emb'], 'L0_rec_social_weight': _L0_rec_in['social_weight']}

def reference(r_users, r_items, L0_rec_user_emb, L0_rec_item_emb, L0_rec_social_weight):
    import jax
    import jax.numpy as jnp

    def _L0_rec_ref(user_emb, item_emb, social_weight, users, items):
        import jax, jax.numpy as jnp
        import numpy as np
        NUM_USERS = 1250
        NUM_ITEMS = 12500
        EMBED_DIM = 64
        BATCH = 512
        bu = user_emb[users]
        bi = item_emb[items]
        pos = jnp.sum(bu * bi, axis=-1)
        social_scores = jnp.einsum('bd,ud->bu', bi, user_emb)
        bw = social_weight[users]
        social_influence = jnp.sum(bw * social_scores, axis=-1)
        return pos + social_influence
    y = _L0_rec_ref(L0_rec_user_emb, L0_rec_item_emb, L0_rec_social_weight, r_users, r_items)
    return y

_drawn_inputs = setup_inputs


def setup_inputs(seed=0):
    import zlib

    import numpy as np

    out = dict(_drawn_inputs(seed))
    spreads = {}
    factors = {}
    for name, (base, spread) in spreads.items():
        noise = np.random.default_rng([zlib.crc32(name.encode()), seed]).standard_normal(out[name].shape)
        drawn = base * np.exp(spread * noise) if base else spread * noise
        out[name] = jnp.asarray(drawn.astype(out[name].dtype))
    for name, factor in factors.items():
        out[name] = (out[name] * factor).astype(out[name].dtype)
    return out
```

```python
import concourse.bass as bass
from concourse import mybir
from contextlib import ExitStack


def build_rec_scores(nc, users, items, user_emb, item_emb, social, out):
    fp32, i32, u32 = mybir.dt.float32, mybir.dt.int32, mybir.dt.uint32
    ALU = mybir.AluOpType
    P = 128
    BATCH = users.shape[0]
    USERS, DIM = user_emb.shape
    ITEMS = item_emb.shape[0]
    TILES = BATCH // P
    UBLK = 125
    UBLKS = USERS // UBLK
    BANK = 512
    SCORE_CHUNKS = [(c, min(BANK, USERS - c)) for c in range(0, USERS, BANK)]
    BANKS = len(SCORE_CHUNKS)

    ctx = ExitStack()
    with ctx:
        def sb(name, shape, dt):
            return ctx.enter_context(nc.sbuf_tensor(name, shape, dt))

        def sem(name):
            return ctx.enter_context(nc.semaphore(name))

        raw_idx = sb("raw_idx", [P, 2, TILES], i32)
        wrap = sb("wrap", [P, 2, TILES], fp32)
        wrapped = sb("wrapped", [P, 2, TILES], fp32)
        idx = sb("idx", [P, 2, TILES], i32)
        ident = sb("ident", [P, P], fp32)
        ones = sb("ones", [P, P], fp32)
        emb = sb("emb", [UBLK, UBLKS, 2, DIM], fp32)
        emb_t = sb("emb_t", [P, USERS], fp32)
        item = sb("item", [P, TILES, 2, DIM], fp32)
        user = sb("user", [P, TILES, DIM], fp32)
        item_t = sb("item_t", [P, TILES, P], fp32)
        rows = sb("rows", [P, TILES, USERS], fp32)
        prod = sb("prod", [P, USERS], fp32)
        pos = sb("pos", [P, TILES], fp32)
        prod_pos = sb("prod_pos", [P, TILES, DIM], fp32)
        soc = sb("soc", [P, TILES], fp32)
        res = sb("res", [P, TILES], fp32)
        scores = [ctx.enter_context(nc.psum_tensor(f"scores{i}", [P, BANKS * BANK], fp32)) for i in range(2)]
        turn = ctx.enter_context(nc.psum_tensor("turn", [P, 2, BANK], fp32))

        idx_in = sem("idx_in")
        emb_in = sem("emb_in")
        wrap_done = sem("wrap_done")
        wrapped_done = sem("wrapped_done")
        idx_ready = sem("idx_ready")
        ones_ready = sem("ones_ready")
        ident_ready = sem("ident_ready")
        item_in = [sem(f"item_in{t}") for t in range(TILES)]
        rows_in = [sem(f"rows_in{t}") for t in range(TILES)]
        user_in = sem("user_in")
        item_dup = sem("item_dup")
        turned = sem("turned")
        unloaded = sem("unloaded")
        scored = sem("scored")
        tile_done = sem("tile_done")
        pp_done = sem("pp_done")
        pos_done = sem("pos_done")
        res_ready = sem("res_ready")
        out_done = sem("out_done")
        EMB_GROUPS = [(0, 4), (4, 8), (8, 10)]
        block = ctx.enter_context(nc.Block())

        @block.sync
        def _(sp):
            sp.dma_start(raw_idx[:, 0, :], items.rearrange("(p t) -> p t", t=TILES)).then_inc(idx_in, 16)
            sp.dma_start(raw_idx[:, 1, :], users.rearrange("(p t) -> p t", t=TILES)).then_inc(idx_in, 16)
            ev = user_emb.rearrange("(k p) d -> p k d", p=UBLK)
            sp.dma_start(emb[:, :, 0, :], ev).then_inc(emb_in, 16)
            sp.dma_start(emb[:, :, 1, :], ev).then_inc(emb_in, 16)
            sp.wait_ge(res_ready, 1)
            sp.dma_start(out.rearrange("(p t) -> p t", t=TILES), res[:, :]).then_inc(out_done, 16)
            sp.wait_ge(out_done, 16)

        @block.gpsimd
        def _(pool):
            nc.gpsimd.memset(ones[:, :], 1.0).then_inc(ones_ready, 1)
            pool.wait_ge(ones_ready, 1)
            nc.gpsimd.affine_select(out=ident[:, :], in_=ones[:, :], pattern=[[-1, P]], compare_op=ALU.is_equal,
                                    fill=0.0, base=0, channel_multiplier=1).then_inc(ident_ready, 1)
            pool.wait_ge(idx_ready, 1)
            for t in range(TILES):
                nc.gpsimd.indirect_dma_start(item[:, t, 0, :], None, item_emb,
                                             bass.IndirectOffsetOnAxis(idx[:, 0, t:t + 1].bitcast(u32), 0)
                                             ).then_inc(item_in[t], 16)
                nc.gpsimd.indirect_dma_start(rows[:, t, :], None, social,
                                             bass.IndirectOffsetOnAxis(idx[:, 1, t:t + 1].bitcast(u32), 0)
                                             ).then_inc(rows_in[t], 16)
            for t in range(TILES):
                nc.gpsimd.indirect_dma_start(user[:, t, :], None, user_emb,
                                             bass.IndirectOffsetOnAxis(idx[:, 1, t:t + 1].bitcast(u32), 0)
                                             ).then_inc(user_in, 16)

        @block.tensor
        def _(pe):
            pe.wait_ge(ident_ready, 1)
            pe.wait_ge(emb_in, 32)
            for g, (lo, hi) in enumerate(EMB_GROUPS):
                if g >= 2:
                    pe.wait_ge(unloaded, g - 1)
                for k in range(lo, hi):
                    last = nc.tensor.transpose(turn[:, g % 2, (k - lo) * UBLK:(k - lo + 1) * UBLK],
                                               emb[:, k, :, :].rearrange("p a d -> p (a d)"),
                                               ident[0:UBLK, 0:UBLK])
                last.then_inc(turned, 1)
            n = len(EMB_GROUPS)
            for t in range(TILES):
                pe.wait_ge(item_dup, t + 1)
                pe.wait_ge(unloaded, n + t - 1)
                nc.tensor.transpose(turn[:, (n + t) % 2, 0:P], item[:, t, :, :].rearrange("p a d -> p (a d)"),
                                    ident[:, :]).then_inc(turned, 1)
                pe.wait_ge(unloaded, n + t + 1)
                if t >= 2:
                    pe.wait_ge(tile_done, t - 1)
                for c, (lo, w) in enumerate(SCORE_CHUNKS):
                    h = (c + t) % 2 * DIM
                    last = nc.tensor.matmul(scores[t % 2][:, lo:lo + w], item_t[h:h + DIM, t, :],
                                            emb_t[h:h + DIM, lo:lo + w], start=True, stop=True)
                last.then_inc(scored, 1)

        @block.scalar
        def _(act):
            for g, (lo, hi) in enumerate(EMB_GROUPS):
                act.wait_ge(turned, g + 1)
                nc.scalar.copy(emb_t[:, lo * UBLK:hi * UBLK], turn[:, g % 2, 0:(hi - lo) * UBLK]).then_inc(unloaded, 1)
            n = len(EMB_GROUPS)
            for t in range(TILES):
                act.wait_ge(item_in[t], 16)
                nc.scalar.copy(item[:, t, 1, :], item[:, t, 0, :]).then_inc(item_dup, 1)
                act.wait_ge(turned, n + t + 1)
                nc.scalar.copy(item_t[:, t, :], turn[:, (n + t) % 2, 0:P]).then_inc(unloaded, 1)

        @block.vector
        def _(dve):
            dve.wait_ge(idx_in, 32)
            for w, n in enumerate((ITEMS, USERS)):
                nc.vector.tensor_scalar(wrap[:, w, :], raw_idx[:, w, :], 0.0, float(n), ALU.is_lt, ALU.mult
                                        ).then_inc(wrap_done, 1)
            dve.wait_ge(wrap_done, 2)
            nc.vector.tensor_tensor(wrapped[:, :, :], raw_idx[:, :, :], wrap[:, :, :], ALU.add
                                    ).then_inc(wrapped_done, 1)
            dve.wait_ge(wrapped_done, 1)
            for w, n in enumerate((ITEMS, USERS)):
                last = nc.vector.tensor_scalar(idx[:, w, :], wrapped[:, w, :], 0.0, float(n - 1), ALU.max, ALU.min)
            last.then_inc(idx_ready, 1)
            for t in range(TILES):
                dve.wait_ge(scored, t + 1)
                dve.wait_ge(rows_in[t], 16)
                if t:
                    dve.wait_ge(tile_done, t)
                nc.vector.tensor_tensor_reduce(out=prod[:, :], in0=scores[t % 2][:, 0:USERS], in1=rows[:, t, :],
                                               scale=1.0, scalar=0.0, op0=ALU.mult, op1=ALU.add,
                                               accum_out=soc[:, t:t + 1]).then_inc(tile_done, 1)
            dve.wait_ge(user_in, 16 * TILES)
            nc.vector.tensor_tensor(prod_pos[:, :, :], item[:, :, 0, :], user[:, :, :], ALU.mult).then_inc(pp_done, 1)
            dve.wait_ge(pp_done, 1)
            nc.vector.reduce_sum(pos[:, :], prod_pos[:, :, :], mybir.AxisListType.X).then_inc(pos_done, 1)
            dve.wait_ge(pos_done, 1)
            dve.wait_ge(tile_done, TILES)
            nc.vector.tensor_tensor(res[:, :], pos[:, :], soc[:, :], ALU.add).then_inc(res_ready, 1)


def kernel(r_users, r_items, L0_rec_user_emb, L0_rec_item_emb, L0_rec_social_weight):
    import numpy as _np
    import concourse.bacc as _bacc
    from concourse import mybir as _mybir
    from concourse.bass_utils import run_bass_kernel_spmd as _run

    nc = _bacc.Bacc("TRN2", target_bir_lowering=False, num_devices=1)
    arrays, args = {}, []
    for name, a in (("users", r_users), ("items", r_items), ("user_emb", L0_rec_user_emb),
                    ("item_emb", L0_rec_item_emb), ("social", L0_rec_social_weight)):
        a = _np.ascontiguousarray(a)
        arrays[name] = a
        args.append(nc.dram_tensor(name, a.shape, _mybir.dt.from_np(a.dtype), kind="ExternalInput").ap())
    args.append(nc.dram_tensor("out", (r_users.shape[0],), _mybir.dt.float32, kind="ExternalOutput").ap())
    build_rec_scores(nc, *args)
    r = _run(nc, [arrays], core_ids=[0])
    return r.results[0]["out"]
```

```python
import concourse.bass as bass
from concourse import mybir
from contextlib import ExitStack


def build_rec_scores(nc, ids, user_emb, item_emb, user_rows, out):
    fp32, bf16, i32, u32 = mybir.dt.float32, mybir.dt.bfloat16, mybir.dt.int32, mybir.dt.uint32
    ALU = mybir.AluOpType
    P = 128
    BATCH = ids.shape[1]
    USERS, DIM = user_emb.shape
    ITEMS = item_emb.shape[0]
    WIDTH = USERS + DIM
    TILES = BATCH // P
    FULL = USERS // P
    REST = USERS - FULL * P
    BLOCKS = FULL + 1
    HALF = BLOCKS // 2
    HALF_COLS = HALF * P
    BANK = 512
    CHUNKS = [(c, min(BANK, WIDTH - c)) for c in range(0, WIDTH, BANK)]
    assert BATCH == TILES * P and BLOCKS == 2 * HALF and 2 * DIM == P

    ctx = ExitStack()
    with ctx:
        def sb(name, shape, dt):
            return ctx.enter_context(nc.sbuf_tensor(name, shape, dt))

        def sem(name):
            return ctx.enter_context(nc.semaphore(name))

        raw_idx = sb("raw_idx", [P, 2, TILES], i32)
        wrap = sb("wrap", [P, 2, TILES], fp32)
        wrapped = sb("wrapped", [P, 2, TILES], fp32)
        idx = sb("idx", [P, 2, TILES], i32)
        ones = sb("ones", [P, BANK], bf16)
        warm = sb("warm", [P, 1], bf16)
        ident = sb("ident", [P, P], bf16)
        emb = sb("emb", [P, BLOCKS, DIM], fp32)
        emb_rest = sb("emb_rest", [P, BLOCKS, DIM], fp32)
        emb_parts = sb("emb_parts", [P, BLOCKS, 3, DIM], bf16)
        moving = sb("moving", [P, 2, WIDTH], bf16)
        item = sb("item", [P, TILES, 4, DIM], fp32)
        item_t = sb("item_t", [P, TILES, 3, P], bf16)
        rows = sb("rows", [P, TILES, WIDTH], fp32)
        prod = sb("prod", [P, WIDTH], fp32)
        res = sb("res", [P, TILES], fp32)
        scores = [ctx.enter_context(nc.psum_tensor(f"scores{i}", [P, len(CHUNKS) * BANK], fp32)) for i in range(2)]
        turn = ctx.enter_context(nc.psum_tensor("turn", [P, 2 * BANK], fp32))
        item_turn = turn[:, :].bitcast(bf16).rearrange("p (a c) -> p a c", a=2)
        emb_turn = [s[:, 0:2 * BANK].bitcast(bf16).rearrange("p (a c) -> p a c", a=2) for s in scores]
        item_parts = item[:, :, :, :].bitcast(bf16).rearrange("p t s (d h) -> p t s d h", h=2)[:, :, :, :, 1]
        HI, MID, HI_AGAIN, LO = range(4)
        WARM = 12
        PASSES = (0, 0, 1)

        ids_in = sem("ids_in")
        tail_zeroed = sem("tail_zeroed")
        emb_in = [sem(f"emb_in{a}") for a in range(2)]
        emb_tail_in = sem("emb_tail_in")
        wrap_done = sem("wrap_done")
        wrapped_done = sem("wrapped_done")
        items_ready = sem("items_ready")
        users_ready = sem("users_ready")
        ones_ready = sem("ones_ready")
        ident_ready = sem("ident_ready")
        ext_ready = sem("ext_ready")
        emb_hi = sem("emb_hi")
        emb_r = sem("emb_r")
        emb_mid = sem("emb_mid")
        emb_lo = sem("emb_lo")
        emb_turned = sem("emb_turned")
        moved_first = sem("moved_first")
        moved_second = sem("moved_second")
        item_in = [sem(f"item_in{t}") for t in range(TILES)]
        rows_in = [sem(f"rows_in{t}") for t in range(TILES)]
        item_r = sem("item_r")
        item_again = sem("item_again")
        item_lo = sem("item_lo")
        item_turned = sem("item_turned")
        item_ready = sem("item_ready")
        scored = sem("scored")
        tile_done = sem("tile_done")
        out_done = sem("out_done")
        block = ctx.enter_context(nc.Block())

        def half(a):
            return slice(a * HALF, (a + 1) * HALF)

        def half_cols(a):
            return slice(a * HALF_COLS, min((a + 1) * HALF_COLS, USERS))

        def load_emb_half(eng, a):
            lo, hi = a * HALF, min((a + 1) * HALF, FULL)
            eng.dma_start(emb[:, lo:hi, :],
                          user_emb[lo * P:hi * P, :].rearrange("(k p) d -> p k d", p=P)).then_inc(emb_in[a], 16)

        @block.sync
        def _(sp):
            sp.dma_start(raw_idx[:, :, :], ids.rearrange("w (p t) -> p w t", t=TILES)).then_inc(ids_in, 16)
            load_emb_half(sp, 1)
            sp.wait_ge(tile_done, TILES)
            sp.dma_start(out.rearrange("(p t) -> p t", t=TILES), res[:, :]).then_inc(out_done, 16)
            sp.wait_ge(out_done, 16)

        @block.gpsimd
        def _(pool):
            nc.gpsimd.memset(ones[:, :], 1.0).then_inc(ones_ready, 1)
            pool.wait_ge(ones_ready, 1)
            nc.gpsimd.affine_select(out=ident[:, :], in_=ones[:, 0:P], pattern=[[-1, P]], compare_op=ALU.is_equal,
                                    fill=0.0, base=0, channel_multiplier=1).then_inc(ident_ready, 1)

            def gather_items(t):
                nc.gpsimd.indirect_dma_start(item[:, t, HI, :], None, item_emb,
                                             bass.IndirectOffsetOnAxis(idx[:, 0, t:t + 1].bitcast(u32), 0)
                                             ).then_inc(item_in[t], 16)

            def gather_rows(t):
                nc.gpsimd.indirect_dma_start(rows[:, t, :], None, user_rows,
                                             bass.IndirectOffsetOnAxis(idx[:, 1, t:t + 1].bitcast(u32), 0)
                                             ).then_inc(rows_in[t], 16)

            pool.wait_ge(items_ready, 1)
            gather_items(0)
            pool.wait_ge(users_ready, 1)
            gather_rows(0)
            gather_items(1)
            for t in range(1, TILES):
                if t + 1 < TILES:
                    gather_items(t + 1)
                gather_rows(t)

        @block.tensor
        def _(pe):
            pe.wait_ge(ones_ready, 1)
            for _ in range(WARM):
                nc.tensor.matmul(turn[:, 0:BANK], ones[:, 0:P], ones[:, :], start=True, stop=True)
            pe.wait_ge(ident_ready, 1)

            def turn_emb(a):
                pe.wait_ge(emb_lo, a + 1)
                for s in range(2):
                    for k in range(a * HALF, (a + 1) * HALF):
                        n = P if k < FULL else REST
                        c = (k - a * HALF) * P
                        last = nc.tensor.transpose(emb_turn[s][:, a, c:c + n],
                                                   emb_parts[0:n, k, 1 - s:3 - s, :].rearrange("p a d -> p (a d)"),
                                                   ident[0:n, 0:n])
                    last.then_inc(emb_turned, 1)

            def turn_item(t):
                pe.wait_ge(item_lo, t + 1)
                pe.wait_ge(item_again, t + 1)
                if t >= 2:
                    pe.wait_ge(item_ready, t - 1)
                for j in range(3):
                    last = nc.tensor.transpose(item_turn[:, t % 2, j * P:(j + 1) * P],
                                               item_parts[:, t, j:j + 2, :].rearrange("p a d -> p (a d)"),
                                               ident[:, :])
                last.then_inc(item_turned, 1)

            turn_emb(0)
            turn_item(0)
            turn_emb(1)
            pe.wait_ge(moved_first, 2)
            pe.wait_ge(moved_second, 2)
            pe.wait_ge(ext_ready, 2)
            for t in range(TILES):
                if t + 1 < TILES:
                    turn_item(t + 1)
                pe.wait_ge(item_ready, t + 1)
                if t >= 2:
                    pe.wait_ge(tile_done, t - 1)
                for j, s in enumerate(PASSES):
                    for lo, n in CHUNKS:
                        last = nc.tensor.matmul(scores[t % 2][:, lo:lo + n], item_t[:, t, j, :],
                                                moving[:, s, lo:lo + n], start=(j == 0), stop=(j == 2))
                last.then_inc(scored, 1)

        @block.scalar
        def _(act):
            load_emb_half(act, 0)
            act.wait_ge(tail_zeroed, 1)
            act.dma_start(emb[0:REST, FULL, :], user_emb[FULL * P:USERS, :]).then_inc(emb_tail_in, 16)
            act.wait_ge(ones_ready, 1)
            nc.scalar.copy(warm[:, :], ones[:, 0:1])
            for a in range(2):
                act.wait_ge(emb_in[a], 16)
                if a == 1:
                    act.wait_ge(emb_tail_in, 16)
                nc.scalar.copy(emb_parts[:, half(a), 1, :], emb[:, half(a), :]).then_inc(emb_hi, 1)
            for a in range(2):
                act.wait_ge(emb_r, a + 1)
                nc.scalar.copy(emb_parts[:, half(a), 2, :], emb_rest[:, half(a), :]).then_inc(emb_mid, 1)

            def repeat_item(t):
                act.wait_ge(item_in[t], 16)
                nc.scalar.copy(item[:, t, HI_AGAIN, :], item[:, t, HI, :]).then_inc(item_again, 1)

            def unload_item(t):
                act.wait_ge(item_turned, t + 1)
                nc.scalar.copy(item_t[:, t, :, :].rearrange("p a b -> p (a b)"),
                               item_turn[:, t % 2, 0:3 * P]).then_inc(item_ready, 1)

            repeat_item(0)
            for a in range(2):
                act.wait_ge(emb_turned, 2 * a + 1)
                cols = half_cols(a)
                nc.scalar.copy(moving[:, 0, cols], emb_turn[0][:, a, 0:cols.stop - cols.start]).then_inc(moved_first, 1)
                if a == 0:
                    unload_item(0)
            for t in range(1, TILES):
                repeat_item(t)
                unload_item(t)

        @block.vector
        def _(dve):
            nc.vector.memset(emb[(REST // 32) * 32:P, FULL, :], 0.0).then_inc(tail_zeroed, 1)
            dve.wait_ge(ids_in, 16)
            for w, n in enumerate((ITEMS, USERS)):
                nc.vector.tensor_scalar(wrap[:, w, :], raw_idx[:, w, :], 0.0, float(n), ALU.is_lt, ALU.mult
                                        ).then_inc(wrap_done, 1)
            dve.wait_ge(wrap_done, 2)
            nc.vector.tensor_tensor(wrapped[:, :, :], raw_idx[:, :, :], wrap[:, :, :], ALU.add
                                    ).then_inc(wrapped_done, 1)
            dve.wait_ge(wrapped_done, 1)
            for w, n, ready in ((0, ITEMS, items_ready), (1, USERS, users_ready)):
                nc.vector.tensor_scalar(idx[:, w, :], wrapped[:, w, :], 0.0, float(n - 1), ALU.max, ALU.min
                                        ).then_inc(ready, 1)
            dve.wait_ge(ident_ready, 1)
            nc.vector.tensor_copy(moving[:, 0, USERS:WIDTH], ident[:, 0:DIM]).then_inc(ext_ready, 1)
            nc.vector.tensor_copy(moving[:, 1, USERS:WIDTH], ident[:, DIM:P]).then_inc(ext_ready, 1)
            for a in range(2):
                dve.wait_ge(emb_hi, a + 1)
                nc.vector.tensor_tensor(emb_rest[:, half(a), :], emb[:, half(a), :], emb_parts[:, half(a), 1, :],
                                        ALU.subtract).then_inc(emb_r, 1)
            for a in range(2):
                dve.wait_ge(emb_r, a + 1)
                dve.wait_ge(emb_mid, a + 1)
                nc.vector.tensor_tensor(emb_parts[:, half(a), 0, :], emb_rest[:, half(a), :],
                                        emb_parts[:, half(a), 2, :], ALU.subtract).then_inc(emb_lo, 1)

            def split_item(t):
                dve.wait_ge(item_in[t], 16)
                nc.vector.tensor_tensor(item[:, t, MID, :], item[:, t, HI, :], item_parts[:, t, HI, :], ALU.subtract
                                        ).then_inc(item_r, 1)
                dve.wait_ge(item_r, t + 1)
                nc.vector.tensor_tensor(item[:, t, LO, :], item[:, t, MID, :], item_parts[:, t, MID, :], ALU.subtract
                                        ).then_inc(item_lo, 1)

            split_item(0)
            for a in range(2):
                dve.wait_ge(emb_turned, 2 * a + 2)
                cols = half_cols(a)
                nc.vector.tensor_copy(moving[:, 1, cols], emb_turn[1][:, a, 0:cols.stop - cols.start]
                                      ).then_inc(moved_second, 1)
            split_item(1)
            for t in range(TILES):
                if t + 2 < TILES:
                    split_item(t + 2)
                dve.wait_ge(scored, t + 1)
                dve.wait_ge(rows_in[t], 16)
                if t:
                    dve.wait_ge(tile_done, t)
                nc.vector.tensor_tensor_reduce(out=prod[:, :], in0=scores[t % 2][:, 0:WIDTH], in1=rows[:, t, :],
                                               scale=1.0, scalar=0.0, op0=ALU.mult, op1=ALU.add,
                                               accum_out=res[:, t:t + 1]).then_inc(tile_done, 1)


def kernel(r_users, r_items, L0_rec_user_emb, L0_rec_item_emb, L0_rec_social_weight):
    import numpy as _np
    import concourse.bacc as _bacc
    from concourse import mybir as _mybir
    from concourse.bass_utils import run_bass_kernel_spmd as _run

    nc = _bacc.Bacc("TRN2", target_bir_lowering=False, num_devices=1)
    user_rows = _np.concatenate([L0_rec_social_weight, L0_rec_user_emb], axis=1)
    ids = _np.stack([r_items, r_users])
    arrays, args = {}, []
    for name, a in (("ids", ids), ("user_emb", L0_rec_user_emb),
                    ("item_emb", L0_rec_item_emb), ("user_rows", user_rows)):
        a = _np.ascontiguousarray(a)
        arrays[name] = a
        args.append(nc.dram_tensor(name, a.shape, _mybir.dt.from_np(a.dtype), kind="ExternalInput").ap())
    args.append(nc.dram_tensor("out", (r_users.shape[0],), _mybir.dt.float32, kind="ExternalOutput").ap())
    build_rec_scores(nc, *args)
    r = _run(nc, [arrays], core_ids=[0])
    return r.results[0]["out"]
```

```python
import concourse.bass as bass
from concourse import mybir
from contextlib import ExitStack


def build_rec_scores(nc, ids, user_emb, item_rows, user_rows, spare, out):
    fp32, bf16, i32, u32 = mybir.dt.float32, mybir.dt.bfloat16, mybir.dt.int32, mybir.dt.uint32
    ALU = mybir.AluOpType
    P = 128
    BATCH = ids.shape[1]
    DIM = user_emb.shape[1]
    USERS = user_rows.shape[0] - spare
    ITEMS = item_rows.shape[0] - spare
    WIDTH = USERS + DIM
    TILES = BATCH // P
    BLOCKS = user_emb.shape[0] // P
    LANES = USERS // BLOCKS
    HALF = BLOCKS // 2
    BANK = 512
    CHUNKS = [(c, min(BANK, WIDTH - c)) for c in range(0, WIDTH, BANK)]
    assert user_rows.shape[1] == WIDTH and spare == P - 1 and USERS == LANES * BLOCKS
    assert BATCH == TILES * P and BLOCKS == 2 * HALF and 2 * DIM == P

    ctx = ExitStack()
    with ctx:
        def sb(name, shape, dt):
            return ctx.enter_context(nc.sbuf_tensor(name, shape, dt))

        def sem(name):
            return ctx.enter_context(nc.semaphore(name))

        raw_idx = sb("raw_idx", [P, 2, TILES], i32)
        lane = sb("lane", [P, 1], i32)
        last_row = sb("last_row", [P, 2], fp32)
        from_end = sb("from_end", [P, 2, TILES], fp32)
        idx = sb("idx", [P, 2, TILES], i32)
        half_idx = sb("half_idx", [P, 2], i32)
        ones = sb("ones", [P, BANK], bf16)
        warm = sb("warm", [P, 1], bf16)
        ident = sb("ident", [P, P], bf16)
        emb = sb("emb", [P, BLOCKS, DIM], fp32)
        emb_rest = sb("emb_rest", [P, BLOCKS, DIM], fp32)
        emb_parts = sb("emb_parts", [P, BLOCKS, 3, DIM], bf16)
        moving = sb("moving", [P, 2, WIDTH], bf16)
        item = sb("item", [P, TILES, 4, DIM], fp32)
        item_t = sb("item_t", [P, TILES, 3, P], bf16)
        rows = sb("rows", [P, TILES, WIDTH], fp32)
        prod = sb("prod", [P, 2, WIDTH], fp32)
        part = sb("part", [P, 1], fp32)
        res = sb("res", [P, TILES], fp32)
        scores = [ctx.enter_context(nc.psum_tensor(f"scores{i}", [P, len(CHUNKS) * BANK], fp32)) for i in range(2)]
        turn = ctx.enter_context(nc.psum_tensor("turn", [P, 2 * BANK], fp32))
        item_turn = turn[:, :].bitcast(bf16).rearrange("p (a c) -> p a c", a=2)
        emb_turn = [s[:, 0:2 * BANK].bitcast(bf16).rearrange("p (a c) -> p a c", a=2) for s in scores]
        item_parts = item[:, :, :, :].bitcast(bf16).rearrange("p t s (d h) -> p t s d h", h=2)[:, :, :, :, 1]
        HI, MID, HI_AGAIN, LO = range(4)
        SPLIT = WIDTH // 2
        half_rows = user_rows.rearrange("u (h w) -> (u h) w", h=2)
        WARM = 12
        PASSES = (0, 0, 1)

        ids_in = sem("ids_in")
        emb_in = [sem(f"emb_in{a}") for a in range(2)]
        lane_ready = sem("lane_ready")
        last_row_ready = sem("last_row_ready")
        from_end_done = sem("from_end_done")
        items_ready = sem("items_ready")
        users_ready = sem("users_ready")
        ones_ready = sem("ones_ready")
        ident_ready = sem("ident_ready")
        ext_ready = sem("ext_ready")
        emb_hi = sem("emb_hi")
        emb_rest_ready = sem("emb_rest_ready")
        emb_mid = sem("emb_mid")
        emb_lo = sem("emb_lo")
        emb_turned = sem("emb_turned")
        moved_first = sem("moved_first")
        moved_second = sem("moved_second")
        item_in = [sem(f"item_in{t}") for t in range(TILES)]
        rows_in = [sem(f"rows_in{t}") for t in range(TILES - 1)]
        item_rest_ready = sem("item_rest_ready")
        item_again = sem("item_again")
        item_lo = sem("item_lo")
        item_turned = sem("item_turned")
        item_ready = sem("item_ready")
        scored = sem("scored")
        half_scored = sem("half_scored")
        half_idx_ready = sem("half_idx_ready")
        half_in = [sem(f"half_in{h}") for h in range(2)]
        part_done = sem("part_done")
        tile_done = sem("tile_done")
        out_done = sem("out_done")
        block = ctx.enter_context(nc.Block())

        def half(a):
            return slice(a * HALF, (a + 1) * HALF)

        def load_emb_half(eng, a):
            eng.dma_start(emb[:, half(a), :],
                          user_emb.rearrange("(p k) d -> p k d", k=BLOCKS)[:, half(a), :]).then_inc(emb_in[a], 16)

        def turned_half(s, a):
            return emb_turn[s][:, a, 0:HALF * P].rearrange("q (k p) -> q k p", p=P)[:, :, 0:LANES]

        def moving_half(s, a):
            return moving[:, s, 0:USERS].rearrange("q (p k) -> q k p", k=BLOCKS)[:, half(a), :]

        @block.sync
        def _(sp):
            sp.dma_start(raw_idx[:, :, :], ids.rearrange("w (p t) -> p w t", t=TILES)).then_inc(ids_in, 16)
            load_emb_half(sp, 1)
            sp.wait_ge(tile_done, TILES)
            sp.dma_start(out.rearrange("(p t) -> p t", t=TILES), res[:, :]).then_inc(out_done, 16)
            sp.wait_ge(out_done, 16)

        @block.gpsimd
        def _(pool):
            nc.gpsimd.iota(lane[:, :], [[0, 1]], base=0, channel_multiplier=1).then_inc(lane_ready, 1)
            nc.gpsimd.memset(ones[:, :], 1.0).then_inc(ones_ready, 1)
            pool.wait_ge(ones_ready, 1)
            nc.gpsimd.affine_select(out=ident[:, :], in_=ones[:, 0:P], pattern=[[-1, P]], compare_op=ALU.is_equal,
                                    fill=0.0, base=0, channel_multiplier=1).then_inc(ident_ready, 1)

            def gather_items(t):
                nc.gpsimd.indirect_dma_start(item[:, t, HI, :], None, item_rows,
                                             bass.IndirectOffsetOnAxis(idx[:, 0, t:t + 1].bitcast(u32), 0)
                                             ).then_inc(item_in[t], 16)

            def gather_rows(t):
                nc.gpsimd.indirect_dma_start(rows[:, t, :], None, user_rows,
                                             bass.IndirectOffsetOnAxis(idx[:, 1, t:t + 1].bitcast(u32), 0)
                                             ).then_inc(rows_in[t], 16)

            pool.wait_ge(items_ready, 1)
            gather_items(0)
            pool.wait_ge(users_ready, 1)
            gather_rows(0)
            gather_items(1)
            gather_rows(1)
            gather_items(2)
            for t in range(2, TILES - 1):
                gather_items(t + 1)
                gather_rows(t)
            pool.wait_ge(half_idx_ready, 2)
            for h in range(2):
                nc.gpsimd.indirect_dma_start(rows[:, TILES - 1, h * SPLIT:(h + 1) * SPLIT], None, half_rows,
                                             bass.IndirectOffsetOnAxis(half_idx[:, h:h + 1].bitcast(u32), 0)
                                             ).then_inc(half_in[h], 16)

        @block.tensor
        def _(pe):
            pe.wait_ge(ones_ready, 1)
            for _ in range(WARM):
                nc.tensor.matmul(turn[:, 0:BANK], ones[:, 0:P], ones[:, :], start=True, stop=True)
            pe.wait_ge(ident_ready, 1)

            def turn_emb(a):
                pe.wait_ge(emb_lo, a + 1)
                for s in range(2):
                    for k in range(a * HALF, (a + 1) * HALF):
                        c = (k - a * HALF) * P
                        last = nc.tensor.transpose(emb_turn[s][:, a, c:c + P],
                                                   emb_parts[:, k, 1 - s:3 - s, :].rearrange("p a d -> p (a d)"),
                                                   ident[:, :])
                    last.then_inc(emb_turned, 1)

            def turn_item(t):
                pe.wait_ge(item_lo, t + 1)
                pe.wait_ge(item_again, t + 1)
                if t >= 2:
                    pe.wait_ge(item_ready, t - 1)
                for j in range(3):
                    last = nc.tensor.transpose(item_turn[:, t % 2, j * P:(j + 1) * P],
                                               item_parts[:, t, j:j + 2, :].rearrange("p a d -> p (a d)"),
                                               ident[:, :])
                last.then_inc(item_turned, 1)

            turn_emb(0)
            turn_item(0)
            turn_emb(1)
            pe.wait_ge(moved_first, 2)
            pe.wait_ge(moved_second, 2)
            pe.wait_ge(ext_ready, 2)
            for t in range(TILES):
                pe.wait_ge(item_ready, t + 1)
                if t >= 2:
                    pe.wait_ge(tile_done, t - 1)
                order = [(j, c) for j in range(3) for c in range(len(CHUNKS))]
                if t == TILES - 1:
                    order.sort(key=lambda jc: jc[1])
                for j, c in order:
                    lo, n = CHUNKS[c]
                    last = nc.tensor.matmul(scores[t % 2][:, lo:lo + n], item_t[:, t, j, :],
                                            moving[:, PASSES[j], lo:lo + n], start=(j == 0), stop=(j == 2))
                    if t == TILES - 1 and j == 2 and lo < SPLIT <= lo + n:
                        last.then_inc(half_scored, 1)
                    if t < TILES - 1 and (j, c) == (0, len(CHUNKS) - 1):
                        turn_item(t + 1)
                last.then_inc(scored, 1)

        @block.scalar
        def _(act):
            load_emb_half(act, 0)
            act.wait_ge(ones_ready, 1)
            nc.scalar.copy(warm[:, :], ones[:, 0:1])
            for a in range(2):
                act.wait_ge(emb_in[a], 16)
                nc.scalar.copy(emb_parts[:, half(a), 1, :], emb[:, half(a), :]).then_inc(emb_hi, 1)
            for a in range(2):
                act.wait_ge(emb_rest_ready, a + 1)
                nc.scalar.copy(emb_parts[:, half(a), 2, :], emb_rest[:, half(a), :]).then_inc(emb_mid, 1)

            def repeat_item(t):
                act.wait_ge(item_in[t], 16)
                nc.scalar.copy(item[:, t, HI_AGAIN, :], item[:, t, HI, :]).then_inc(item_again, 1)

            def unload_item(t):
                act.wait_ge(item_turned, t + 1)
                nc.scalar.copy(item_t[:, t, :, :].rearrange("p a b -> p (a b)"),
                               item_turn[:, t % 2, 0:3 * P]).then_inc(item_ready, 1)

            repeat_item(0)
            for a in range(2):
                act.wait_ge(emb_turned, 2 * a + 1)
                nc.scalar.copy(moving_half(0, a), turned_half(0, a)).then_inc(moved_first, 1)
                if a == 0:
                    unload_item(0)
            for t in range(1, TILES):
                repeat_item(t)
                unload_item(t)

        @block.vector
        def _(dve):
            dve.wait_ge(lane_ready, 1)
            for w, n in enumerate((ITEMS, USERS)):
                nc.vector.tensor_scalar(last_row[:, w:w + 1], lane[:, :], float(n - 1), None, ALU.add
                                        ).then_inc(last_row_ready, 1)
            dve.wait_ge(ids_in, 16)
            for w, n in enumerate((ITEMS, USERS)):
                nc.vector.tensor_scalar(from_end[:, w, :], raw_idx[:, w, :], float(n), 0.0, ALU.add, ALU.max
                                        ).then_inc(from_end_done, 1)
            for w, ready in enumerate((items_ready, users_ready)):
                dve.wait_ge(last_row_ready, w + 1)
                dve.wait_ge(from_end_done, w + 1)
                nc.vector.scalar_tensor_tensor(idx[:, w, :], raw_idx[:, w, :].bitcast(u32), last_row[:, w:w + 1],
                                               from_end[:, w, :], ALU.min, ALU.min).then_inc(ready, 1)
            dve.wait_ge(users_ready, 1)
            for h in range(2):
                nc.vector.tensor_scalar(half_idx[:, h:h + 1], idx[:, 1, TILES - 1:TILES], 2.0, float(h),
                                        ALU.mult, ALU.add).then_inc(half_idx_ready, 1)
            dve.wait_ge(ident_ready, 1)
            nc.vector.tensor_copy(moving[:, 0, USERS:WIDTH], ident[:, 0:DIM]).then_inc(ext_ready, 1)
            nc.vector.tensor_copy(moving[:, 1, USERS:WIDTH], ident[:, DIM:P]).then_inc(ext_ready, 1)
            for a in range(2):
                dve.wait_ge(emb_hi, a + 1)
                nc.vector.tensor_tensor(emb_rest[:, half(a), :], emb[:, half(a), :], emb_parts[:, half(a), 1, :],
                                        ALU.subtract).then_inc(emb_rest_ready, 1)
            for a in range(2):
                dve.wait_ge(emb_rest_ready, a + 1)
                dve.wait_ge(emb_mid, a + 1)
                nc.vector.tensor_tensor(emb_parts[:, half(a), 0, :], emb_rest[:, half(a), :],
                                        emb_parts[:, half(a), 2, :], ALU.subtract).then_inc(emb_lo, 1)

            def split_item(t):
                dve.wait_ge(item_in[t], 16)
                nc.vector.tensor_tensor(item[:, t, MID, :], item[:, t, HI, :], item_parts[:, t, HI, :], ALU.subtract
                                        ).then_inc(item_rest_ready, 1)
                dve.wait_ge(item_rest_ready, t + 1)
                nc.vector.tensor_tensor(item[:, t, LO, :], item[:, t, MID, :], item_parts[:, t, MID, :], ALU.subtract
                                        ).then_inc(item_lo, 1)

            split_item(0)
            for a in range(2):
                dve.wait_ge(emb_turned, 2 * a + 2)
                nc.vector.tensor_copy(moving_half(1, a), turned_half(1, a)).then_inc(moved_second, 1)
            split_item(1)
            for t in range(TILES - 1):
                if t + 2 < TILES:
                    split_item(t + 2)
                dve.wait_ge(scored, t + 1)
                dve.wait_ge(rows_in[t], 16)
                if t >= 2:
                    dve.wait_ge(tile_done, t - 1)
                nc.vector.tensor_tensor_reduce(out=prod[:, t % 2, :], in0=scores[t % 2][:, 0:WIDTH], in1=rows[:, t, :],
                                               scale=1.0, scalar=0.0, op0=ALU.mult, op1=ALU.add,
                                               accum_out=res[:, t:t + 1]).then_inc(tile_done, 1)
            t = TILES - 1
            dve.wait_ge(half_scored, 1)
            dve.wait_ge(half_in[0], 16)
            dve.wait_ge(tile_done, t - 1)
            nc.vector.tensor_tensor_reduce(out=prod[:, t % 2, 0:SPLIT], in0=scores[t % 2][:, 0:SPLIT],
                                           in1=rows[:, t, 0:SPLIT], scale=1.0, scalar=0.0, op0=ALU.mult, op1=ALU.add,
                                           accum_out=part[:, :]).then_inc(part_done, 1)
            dve.wait_ge(part_done, 1)
            dve.wait_ge(scored, t + 1)
            dve.wait_ge(half_in[1], 16)
            nc.vector.tensor_tensor_reduce(out=prod[:, t % 2, SPLIT:WIDTH], in0=scores[t % 2][:, SPLIT:WIDTH],
                                           in1=rows[:, t, SPLIT:WIDTH], scale=1.0, scalar=part[:, :],
                                           op0=ALU.mult, op1=ALU.add,
                                           accum_out=res[:, t:t + 1]).then_inc(tile_done, 1)


def kernel(r_users, r_items, L0_rec_user_emb, L0_rec_item_emb, L0_rec_social_weight):
    import numpy as _np
    import concourse.bacc as _bacc
    from concourse import mybir as _mybir
    from concourse.bass_utils import run_bass_kernel_spmd as _run

    nc = _bacc.Bacc("TRN2", target_bir_lowering=False, num_devices=1)
    user_rows = _np.concatenate([L0_rec_social_weight, L0_rec_user_emb], axis=1)
    spare = 127
    user_rows = _np.concatenate([user_rows] + [user_rows[-1:]] * spare)
    item_rows = _np.concatenate([L0_rec_item_emb] + [L0_rec_item_emb[-1:]] * spare)
    user_emb = _np.concatenate([L0_rec_user_emb] + [L0_rec_user_emb[-1:]] * (-L0_rec_user_emb.shape[0] % 128))
    ids = _np.stack([r_items, r_users])
    arrays, args = {}, []
    for name, a in (("ids", ids), ("user_emb", user_emb),
                    ("item_rows", item_rows), ("user_rows", user_rows)):
        a = _np.ascontiguousarray(a)
        arrays[name] = a
        args.append(nc.dram_tensor(name, a.shape, _mybir.dt.from_np(a.dtype), kind="ExternalInput").ap())
    args.append(spare)
    args.append(nc.dram_tensor("out", (r_users.shape[0],), _mybir.dt.float32, kind="ExternalOutput").ap())
    build_rec_scores(nc, *args)
    r = _run(nc, [arrays], core_ids=[0])
    return r.results[0]["out"]
```
